# Optimizing a Trainium2 kernel written in Bass

```python
import numpy as np
import jax
import jax.numpy as jnp

def _softmax(x, axis=-1):
    return jax.nn.softmax(x, axis=axis)

def _gelu(x):
    return jax.nn.gelu(x, approximate=True)

def _silu(x):
    return jax.nn.silu(x)

def _sigmoid(x):
    return jax.nn.sigmoid(x)

def _layernorm(x, axis=-1, eps=1e-05):
    m = jnp.mean(x, axis=axis, keepdims=True)
    v = jnp.var(x, axis=axis, keepdims=True)
    return (x - m) / jnp.sqrt(v + eps)

def _scatter_add(tgt, idx, src, axis=0):
    return tgt.at[idx].add(src)

def _segment_sum(src, seg, n):
    return jax.ops.segment_sum(src, seg, n)
kernel_name = 'mk_dlrm_tower_d1_rec_r8_7bd7f4'

def setup_inputs(seed: int=0):
    np.random.seed(seed)
    _w = jnp.asarray

    def _rec_inputs():
        import jax
        import jax.numpy as jnp
        _tk = jax.random.key(seed)
        ids = jnp.stack([jax.random.randint(jax.random.fold_in(_tk, 200 + f), (2048,), 0, v, jnp.int32) for f, v in enumerate([125000, 12500, 12500, 12500, 12500, 1000, 12500, 12500, 12500, 1000, 12500, 1000, 1000, 1250, 1250, 12500, 1000, 1250, 1000, 1250, 1000, 1000, 1000, 1000, 1000, 1000])], axis=1)
        tbl_0 = 0.05 * jax.random.normal(jax.random.fold_in(_tk, 500 + 0), (125000, 128), jnp.float32)
        tbl_1 = 0.05 * jax.random.normal(jax.random.fold_in(_tk, 500 + 1), (12500, 128), jnp.float32)
        tbl_2 = 0.05 * jax.random.normal(jax.random.fold_in(_tk, 500 + 2), (12500, 128), jnp.float32)
        tbl_3 = 0.05 * jax.random.normal(jax.random.fold_in(_tk, 500 + 3), (12500, 128), jnp.float32)
        tbl_4 = 0.05 * jax.random.normal(jax.random.fold_in(_tk, 500 + 4), (12500, 128), jnp.float32)
        tbl_5 = 0.05 * jax.random.normal(jax.random.fold_in(_tk, 500 + 5), (1000, 128), jnp.float32)
        tbl_6 = 0.05 * jax.random.normal(jax.random.fold_in(_tk, 500 + 6), (12500, 128), jnp.float32)
        tbl_7 = 0.05 * jax.random.normal(jax.random.fold_in(_tk, 500 + 7), (12500, 128), jnp.float32)
        tbl_8 = 0.05 * jax.random.normal(jax.random.fold_in(_tk, 500 + 8), (12500, 128), jnp.float32)
        tbl_9 = 0.05 * jax.random.normal(jax.random.fold_in(_tk, 500 + 9), (1000, 128), jnp.float32)
        tbl_10 = 0.05 * jax.random.normal(jax.random.fold_in(_tk, 500 + 10), (12500, 128), jnp.float32)
        tbl_11 = 0.05 * jax.random.normal(jax.random.fold_in(_tk, 500 + 11), (1000, 128), jnp.float32)
        tbl_12 = 0.05 * jax.random.normal(jax.random.fold_in(_tk, 500 + 12), (1000, 128), jnp.float32)
        tbl_13 = 0.05 * jax.random.normal(jax.random.fold_in(_tk, 500 + 13), (1250, 128), jnp.float32)
        tbl_14 = 0.05 * jax.random.normal(jax.random.fold_in(_tk, 500 + 14), (1250, 128), jnp.float32)
        tbl_15 = 0.05 * jax.random.normal(jax.random.fold_in(_tk, 500 + 15), (12500, 128), jnp.float32)
        tbl_16 = 0.05 * jax.random.normal(jax.random.fold_in(_tk, 500 + 16), (1000, 128), jnp.float32)
        tbl_17 = 0.05 * jax.random.normal(jax.random.fold_in(_tk, 500 + 17), (1250, 128), jnp.float32)
        tbl_18 = 0.05 * jax.random.normal(jax.random.fold_in(_tk, 500 + 18), (1000, 128), jnp.float32)
        tbl_19 = 0.05 * jax.random.normal(jax.random.fold_in(_tk, 500 + 19), (1250, 128), jnp.float32)
        tbl_20 = 0.05 * jax.random.normal(jax.random.fold_in(_tk, 500 + 20), (1000, 128), jnp.float32)
        tbl_21 = 0.05 * jax.random.normal(jax.random.fold_in(_tk, 500 + 21), (1000, 128), jnp.float32)
        tbl_22 = 0.05 * jax.random.normal(jax.random.fold_in(_tk, 500 + 22), (1000, 128), jnp.float32)
        tbl_23 = 0.05 * jax.random.normal(jax.random.fold_in(_tk, 500 + 23), (1000, 128), jnp.float32)
        tbl_24 = 0.05 * jax.random.normal(jax.random.fold_in(_tk, 500 + 24), (1000, 128), jnp.float32)
        tbl_25 = 0.05 * jax.random.normal(jax.random.fold_in(_tk, 500 + 25), (1000, 128), jnp.float32)
        _rk = jax.random.fold_in(_tk, 7)
        r_dense_features = -0.000520686 + 1.00062 * jax.random.normal(jax.random.fold_in(_rk, 101), (2048, 128), jnp.float32)
        W_top1 = 0.0405887 * jax.random.normal(jax.random.fold_in(_tk, 801), (607, 512), jnp.float32)
        W_top2 = 0.0441942 * jax.random.normal(jax.random.fold_in(_tk, 802), (512, 256), jnp.float32)
        W_top3 = 0.0625 * jax.random.normal(jax.random.fold_in(_tk, 803), (256, 1), jnp.float32)
        b_top1 = jnp.zeros((512,), jnp.float32)
        b_top2 = jnp.zeros((256,), jnp.float32)
        return (r_dense_features, ids, tbl_0, tbl_1, tbl_2, tbl_3, tbl_4, tbl_5, tbl_6, tbl_7, tbl_8, tbl_9, tbl_10, tbl_11, tbl_12, tbl_13, tbl_14, tbl_15, tbl_16, tbl_17, tbl_18, tbl_19, tbl_20, tbl_21, tbl_22, tbl_23, tbl_24, tbl_25, W_top1, b_top1, W_top2, b_top2, W_top3)
    r_dense_features, ids, tbl_0, tbl_1, tbl_2, tbl_3, tbl_4, tbl_5, tbl_6, tbl_7, tbl_8, tbl_9, tbl_10, tbl_11, tbl_12, tbl_13, tbl_14, tbl_15, tbl_16, tbl_17, tbl_18, tbl_19, tbl_20, tbl_21, tbl_22, tbl_23, tbl_24, tbl_25, W_top1, b_top1, W_top2, b_top2, W_top3 = _rec_inputs()

    def _L0_rec_setup():
        import jax, jax.numpy as jnp
        import numpy as np
        B, F, D = (2048, 26, 128)
        key = jax.random.key(seed)
        k1, k2 = jax.random.split(key)
        dense_features = jax.random.normal(k1, (B, D), dtype=jnp.float32)
        sparse_values = jax.random.normal(k2, (B, F, D), dtype=jnp.float32)
        return {'dense_features': dense_features, 'sparse_values': sparse_values}
    _L0_rec_all = _L0_rec_setup()
    _L0_rec_in = {k: v for k, v in _L0_rec_all.items() if k in ()}
    del _L0_rec_all
    return {'r_dense_features': r_dense_features, 'ids': ids, 'tbl_0': tbl_0, 'tbl_1': tbl_1, 'tbl_2': tbl_2, 'tbl_3': tbl_3, 'tbl_4': tbl_4, 'tbl_5': tbl_5, 'tbl_6': tbl_6, 'tbl_7': tbl_7, 'tbl_8': tbl_8, 'tbl_9': tbl_9, 'tbl_10': tbl_10, 'tbl_11': tbl_11, 'tbl_12': tbl_12, 'tbl_13': tbl_13, 'tbl_14': tbl_14, 'tbl_15': tbl_15, 'tbl_16': tbl_16, 'tbl_17': tbl_17, 'tbl_18': tbl_18, 'tbl_19': tbl_19, 'tbl_20': tbl_20, 'tbl_21': tbl_21, 'tbl_22': tbl_22, 'tbl_23': tbl_23, 'tbl_24': tbl_24, 'tbl_25': tbl_25, 'W_top1': W_top1, 'b_top1': b_top1, 'W_top2': W_top2, 'b_top2': b_top2, 'W_top3': W_top3}

def reference(r_dense_features, ids, tbl_0, tbl_1, tbl_2, tbl_3, tbl_4, tbl_5, tbl_6, tbl_7, tbl_8, tbl_9, tbl_10, tbl_11, tbl_12, tbl_13, tbl_14, tbl_15, tbl_16, tbl_17, tbl_18, tbl_19, tbl_20, tbl_21, tbl_22, tbl_23, tbl_24, tbl_25, W_top1, b_top1, W_top2, b_top2, W_top3):
    import jax
    import jax.numpy as jnp

    def _L0_rec_ref(dense_features, sparse_values):
        import jax, jax.numpy as jnp
        import numpy as np
        B, F, D = (2048, 26, 128)
        sd = jnp.einsum('bfd,bd->bf', sparse_values, dense_features)
        ss = jnp.einsum('bfd,bgd->bfg', sparse_values, sparse_values)
        iu, ju = jnp.triu_indices(F, k=1)
        pairs = ss[:, iu, ju]
        return jnp.concatenate([dense_features, sd, pairs], axis=1)
    e = jnp.stack([tbl_0[ids[:, 0]], tbl_1[ids[:, 1]], tbl_2[ids[:, 2]], tbl_3[ids[:, 3]], tbl_4[ids[:, 4]], tbl_5[ids[:, 5]], tbl_6[ids[:, 6]], tbl_7[ids[:, 7]], tbl_8[ids[:, 8]], tbl_9[ids[:, 9]], tbl_10[ids[:, 10]], tbl_11[ids[:, 11]], tbl_12[ids[:, 12]], tbl_13[ids[:, 13]], tbl_14[ids[:, 14]], tbl_15[ids[:, 15]], tbl_16[ids[:, 16]], tbl_17[ids[:, 17]], tbl_18[ids[:, 18]], tbl_19[ids[:, 19]], tbl_20[ids[:, 20]], tbl_21[ids[:, 21]], tbl_22[ids[:, 22]], tbl_23[ids[:, 23]], tbl_24[ids[:, 24]], tbl_25[ids[:, 25]]], axis=1)
    z = _L0_rec_ref(r_dense_features, e)
    z = z.reshape(z.shape[0], -1)
    h = jnp.concatenate([z, r_dense_features], axis=1)
    h = jnp.maximum(h @ W_top1 + b_top1, 0.0)
    h = jnp.maximum(h @ W_top2 + b_top2, 0.0)
    y = h @ W_top3
    return y

_drawn_inputs = setup_inputs


def setup_inputs(seed=0):
    import zlib

    import numpy as np

    out = dict(_drawn_inputs(seed))
    spreads = {'b_top1': (0.0, 0.1), 'b_top2': (0.0, 0.1)}
    factors = {}
    for name, (base, spread) in spreads.items():
        noise = np.random.default_rng([zlib.crc32(name.encode()), seed]).standard_normal(out[name].shape)
        drawn = base * np.exp(spread * noise) if base else spread * noise
        out[name] = jnp.asarray(drawn.astype(out[name].dtype))
    for name, factor in factors.items():
        out[name] = (out[name] * factor).astype(out[name].dtype)
    return out
```

```python
import concourse.bass as bass
from concourse import mybir
from contextlib import ExitStack

FEATURES = 26


def dlrm_tower(nc: bass.Bass, dense, ids, tables, w_pairs, w_top1, b_top1, w_top2, b_top2, w_top3, out):
    fp32, i32 = mybir.dt.float32, mybir.dt.int32
    ALU = mybir.AluOpType
    ACT = mybir.ActivationFunctionType

    B, D = dense.shape
    F = FEATURES
    V = F + 1
    VP = 32
    P = 128
    SUPER = 512
    NSUPER = B // SUPER
    SUB = SUPER // P
    S = P // VP
    GROUPS = SUPER // S
    SUBGROUPS = P // S
    BATCH = 8
    BATCHES = SUBGROUPS // BATCH
    NPAIR = V * (V - 1) // 2
    KT = 3
    KR = NPAIR // KT
    H1 = w_top1.shape[1]
    H2 = w_top2.shape[1]
    J1, J2 = H1 // P, H2 // P
    TGROUPS = [list(range(v, min(v + 4, V))) for v in range(0, V, 4)]
    NT = len(TGROUPS)
    FILLS = J1 + J2 + 1

    PIECES, row = [], 0
    for k in range(1, V):
        f = 0
        while f < V - k:
            n = min(V - k - f, KR - row % KR)
            PIECES.append((k, f, n, row // KR, row % KR))
            f, row = f + n, row + n
    assert row == NPAIR

    products = nc.dram_tensor("products", (NSUPER, V * V, S, GROUPS), fp32, kind="Internal").ap()

    ctx = ExitStack()
    with ctx:
        def sb(name, shape, dt=fp32):
            return ctx.enter_context(nc.sbuf_tensor(name, shape, dt))

        def pb(name, shape):
            return ctx.enter_context(nc.psum_tensor(name, shape, fp32))

        def sem(name):
            return ctx.enter_context(nc.semaphore(name))

        index = sb("index", [P, SUB, F], i32)
        rows = [sb(f"rows{q}", [P, V, D]) for q in range(SUB)]
        vecT = [sb(f"vecT{i}", [D, P, VP]) for i in range(2)]
        denseT = sb("denseT", [D, S, GROUPS])
        gram = sb("gram", [P, V, GROUPS])
        pairs = sb("pairs", [KR, KT, SUPER])
        ident = sb("ident", [P, P])
        w1p = sb("w1p", [KR, KT, H1])
        w1a = sb("w1a", [D, H1])
        w1b = sb("w1b", [D, H1])
        w1d = sb("w1d", [D, H1])
        b1 = sb("b1", [P, J1])
        w2 = sb("w2", [P, J1, H2])
        b2 = sb("b2", [P, J2])
        w3 = sb("w3", [P, J2])
        hid1 = sb("hid1", [P, J1, SUPER])
        hid2 = sb("hid2", [P, J2, SUPER])
        y = sb("y", [1, SUPER])

        psT = [pb(f"psT{i}", [P, 4, P]) for i in range(2)]
        psG = [pb(f"psG{i}", [P, 2, 512]) for i in range(2)]
        psM = [pb(f"psM{i}", [P, SUPER]) for i in range(2)]

        ident_zero = sem("ident_zero")
        ident_ready = sem("ident_ready")
        pad_ready = sem("pad_ready")
        w_loaded = sem("w_loaded")
        wd_ready = sem("wd_ready")
        gathers_started = sem("gathers_started")
        index_ready = [sem(f"index_ready{q}") for q in range(SUB)]
        dense_ready = [sem(f"dense_ready{q}") for q in range(SUB)]
        rows_ready = [[sem(f"rows_ready{q}_{t}") for t in range(NT)] for q in range(SUB)]
        t_full = [sem(f"t_full{i}") for i in range(2)]
        t_copied = [sem(f"t_copied{i}") for i in range(2)]
        gram_full = [sem(f"gram_full{i}") for i in range(2)]
        gram_copied = [sem(f"gram_copied{i}") for i in range(2)]
        gram_stored = sem("gram_stored")
        pairs_ready = sem("pairs_ready")
        mlp_full = sem("mlp_full")
        mlp_copied = sem("mlp_copied")
        y_stored = sem("y_stored")

        T_IN = [len(range(i, NT, 2)) for i in range(2)]
        G_IN = BATCHES // 2
        WEIGHTS = 7

        block = ctx.enter_context(nc.Block())

        def over_superchunks(eng, body):
            body(0)
            with eng.Fori(1, NSUPER) as c:
                body(c)

        @block.gpsimd
        def _(pool):
            def superchunk(c):
                for q in range(SUB):
                    if not isinstance(c, int):
                        pool.wait_ge(t_full[(NT - 1) % 2], T_IN[(NT - 1) % 2] * (SUB * (c - 1) + q + 1))
                    pool.wait_ge(index_ready[q], 16 * (c + 1))
                    if not isinstance(c, int):
                        pool.sem_inc(gathers_started, 1)
                    for f in range(F):
                        pool.indirect_dma_start(
                            out=rows[q][:, f, :], out_offset=None, in_=tables[f],
                            in_offset=bass.IndirectOffsetOnAxis(ap=index[:, q, f:f + 1], axis=0),
                        ).then_inc(rows_ready[q][f // 4], 16)
                    if isinstance(c, int) and q == 0:
                        pool.memset(ident[:, :], 0.0).then_inc(ident_zero, 1)
                        pool.wait_ge(ident_zero, 1)
                        pool.affine_select(out=ident[:, :], in_=ident[:, :], compare_op=ALU.not_equal, fill=1.0,
                                           base=0, pattern=[[-1, P]], channel_multiplier=1).then_inc(ident_ready, 1)

            over_superchunks(pool, superchunk)

        @block.sync
        def _(sp):
            def load_inputs(c, q):
                if not isinstance(c, int):
                    sp.wait_ge(t_full[(NT - 1) % 2], T_IN[(NT - 1) % 2] * (SUB * (c - 1) + q + 1))
                at = c * SUPER + q * P
                sp.dma_start(index[:, q, :], ids[bass.ds(at, P), :]).then_inc(index_ready[q], 16)
                sp.dma_start(rows[q][:, F, :], dense[bass.ds(at, P), :]).then_inc(dense_ready[q], 16)

            def load_weights():
                sp.dma_start(w1p[:, :, :], w_pairs.rearrange("(t r) n -> r t n", r=KR)).then_inc(w_loaded, 16)
                sp.dma_start(w1a[:, :], w_top1[0:D, :]).then_inc(w_loaded, 16)
                sp.dma_start(w1b[:, :], w_top1[D + NPAIR:, :]).then_inc(w_loaded, 16)
                sp.dma_start(w2[:, :, :], w_top2.rearrange("(t p) n -> p t n", p=P)).then_inc(w_loaded, 16)
                sp.dma_start(b1[:, :], b_top1).then_inc(w_loaded, 16)
                sp.dma_start(b2[:, :], b_top2).then_inc(w_loaded, 16)
                sp.dma_start(w3[:, :], w_top3).then_inc(w_loaded, 16)

            def superchunk(c):
                for q in range(SUB):
                    load_inputs(c, q)
                if isinstance(c, int):
                    load_weights()
                for i in range(2):
                    sp.wait_ge(gram_copied[i], SUB * G_IN * (c + 1))
                for s in range(S):
                    sp.dma_start(products[c, :, s, :].rearrange("(f g) n -> f g n", f=V),
                                 gram[VP * s:VP * s + V, :, :]).then_inc(gram_stored, 16)
                sp.wait_ge(gram_stored, 16 * S * (c + 1))
                if not isinstance(c, int):
                    sp.wait_ge(mlp_full, FILLS * (c - 1) + J1)
                for k, f, n, t, r in PIECES:
                    first = f * (V + 1) + k
                    sp.dma_start(pairs[r:r + n, t, :],
                                 products[c, first:first + (n - 1) * (V + 1) + 1:V + 1, :, :]
                                 .rearrange("r s n -> r (s n)")).then_inc(pairs_ready, 16)

            over_superchunks(sp, superchunk)

        def copy_vectors(eng, copy, c, q, t):
            i = t % 2
            n = SUB * c + q
            eng.wait_ge(t_full[i], T_IN[i] * n + t // 2 + 1)
            if not isinstance(c, int) or q >= 2:
                for g in range(2):
                    eng.wait_ge(gram_full[g], G_IN * (n - 1))
            vs = TGROUPS[t]
            return copy(vecT[q % 2][:, :, vs[0]:vs[-1] + 1].rearrange("d b v -> d v b"), psT[i][:, 0:len(vs), :])

        def copy_products(eng, copy, c, q, h):
            i = h % 2
            n = SUB * c + q
            eng.wait_ge(gram_full[i], G_IN * n + h // 2 + 1)
            at = q * SUBGROUPS + h * BATCH
            for s in range(S):
                last = copy(gram[VP * s:VP * s + V, :, at:at + BATCH].rearrange("f g (b n) -> f b n g", b=2),
                            psG[i][VP * s:VP * s + V, :, 0:4 * S * V]
                            .rearrange("f b (n s g) -> f b n s g", n=4, s=S)[:, :, :, s, :])
            return last

        @block.scalar
        def _(act):
            def copy(o, i):
                return act.activation(o, i, ACT.Copy)

            def superchunk(c):
                for q in range(SUB):
                    for t in range(0, NT, 2):
                        if t == NT - 1:
                            act.wait_ge(t_full[0], T_IN[0] * (SUB * c + q) + t // 2 + 1)
                            act.activation(denseT[:, :, q * SUBGROUPS:(q + 1) * SUBGROUPS],
                                           psT[0][:, F % 4, :].rearrange("d (n s) -> d s n", s=S), ACT.Copy)
                        copy_vectors(act, copy, c, q, t).then_inc(t_copied[0], 1)
                    for h in range(1, BATCHES, 2):
                        if q == 0 and h == 1 and not isinstance(c, int):
                            act.wait_ge(gram_stored, 16 * S * c)
                        copy_products(act, copy, c, q, h).then_inc(gram_copied[1], 1)
                if isinstance(c, int):
                    act.wait_ge(w_loaded, 16 * WEIGHTS)
                for j in range(J1):
                    act.wait_ge(mlp_full, FILLS * c + j + 1)
                    act.activation(hid1[:, j, :], psM[j % 2][:, :], ACT.Relu, bias=b1[:, j:j + 1]).then_inc(mlp_copied, 1)
                for j in range(J2):
                    act.wait_ge(mlp_full, FILLS * c + J1 + j + 1)
                    act.activation(hid2[:, j, :], psM[j % 2][:, :], ACT.Relu, bias=b2[:, j:j + 1]).then_inc(mlp_copied, 1)
                act.wait_ge(mlp_full, FILLS * (c + 1))
                if not isinstance(c, int):
                    act.wait_ge(y_stored, 16 * c)
                act.activation(y[:, :].rearrange("o (n s) -> o s n", s=S),
                               psM[0][0:1, :].rearrange("o (s n) -> o s n", s=S), ACT.Copy).then_inc(mlp_copied, 1)
                act.wait_ge(mlp_copied, FILLS * (c + 1))
                act.dma_start(out[bass.ds(c * SUPER, SUPER), :].rearrange("b o -> o b"), y[:, :]).then_inc(y_stored, 16)

            over_superchunks(act, superchunk)
            act.wait_ge(y_stored, 16 * NSUPER)

        @block.vector
        def _(dve):
            def copy(o, i):
                return dve.tensor_copy(o, i)

            for i in range(2):
                dve.memset(vecT[i][:, :, V:VP], 0.0).then_inc(pad_ready, 1)

            def superchunk(c):
                for q in range(SUB):
                    for t in range(1, NT, 2):
                        copy_vectors(dve, copy, c, q, t).then_inc(t_copied[1], 1)
                    for h in range(0, BATCHES, 2):
                        if q == 0 and h == 0 and not isinstance(c, int):
                            dve.wait_ge(gram_stored, 16 * S * c)
                        copy_products(dve, copy, c, q, h).then_inc(gram_copied[0], 1)
                if isinstance(c, int):
                    dve.wait_ge(w_loaded, 16 * WEIGHTS)
                    dve.tensor_tensor(w1d[:, :], w1a[:, :], w1b[:, :], ALU.add).then_inc(wd_ready, 1)

            over_superchunks(dve, superchunk)

        @block.tensor
        def _(pe):
            def superchunk(c):
                for q in range(SUB):
                    n = SUB * c + q
                    for t, vs in enumerate(TGROUPS):
                        i = t % 2
                        pe.wait_ge(rows_ready[q][t], 16 * len([v for v in vs if v < F]) * (c + 1))
                        if F in vs:
                            pe.wait_ge(dense_ready[q], 16 * (c + 1))
                        if isinstance(c, int) and q == 0 and t == 0:
                            pe.wait_ge(ident_ready, 1)
                        if not (isinstance(c, int) and q == 0 and t < 2):
                            pe.wait_ge(t_copied[i], T_IN[i] * n + t // 2)
                        for v in vs:
                            last = pe.transpose(psT[i][:, v % 4, :], rows[q][:, v, :], ident[:, :])
                        last.then_inc(t_full[i], 1)
                    for i in range(2):
                        pe.wait_ge(t_copied[i], T_IN[i] * (n + 1))
                    if isinstance(c, int) and q == 0:
                        pe.wait_ge(pad_ready, 2)
                    vec = vecT[q % 2]
                    for h in range(BATCHES):
                        i = h % 2
                        if not (isinstance(c, int) and q == 0 and h < 2):
                            pe.wait_ge(gram_copied[i], G_IN * n + h // 2)
                        for g in range(BATCH):
                            at = (h * BATCH + g) * S
                            last = pe.matmul(psG[i][:, g // 4, g % 4 * S * V:(g % 4 + 1) * S * V],
                                             vec[:, at:at + S, :], vec[:, at:at + S, 0:V], start=True, stop=True)
                        last.then_inc(gram_full[i], 1)
                if isinstance(c, int):
                    pe.wait_ge(w_loaded, 16 * WEIGHTS)
                    pe.wait_ge(wd_ready, 1)
                pe.wait_ge(pairs_ready, 16 * len(PIECES) * (c + 1))
                for j in range(J1):
                    if j >= 2:
                        pe.wait_ge(mlp_copied, FILLS * c + j - 1)
                    elif not isinstance(c, int):
                        pe.wait_ge(mlp_copied, FILLS * c)
                    pe.matmul(psM[j % 2][:, :], w1d[:, j * P:(j + 1) * P],
                              denseT[:, :, :].rearrange("d s n -> d (s n)"), start=True, stop=False)
                    for t in range(KT):
                        last = pe.matmul(psM[j % 2][:, :], w1p[:, t, j * P:(j + 1) * P], pairs[:, t, :],
                                         start=False, stop=t == KT - 1)
                    last.then_inc(mlp_full, 1)
                for j in range(J2):
                    pe.wait_ge(mlp_copied, FILLS * c + J1)
                    for t in range(J1):
                        last = pe.matmul(psM[j % 2][:, :], w2[:, t, j * P:(j + 1) * P], hid1[:, t, :],
                                         start=t == 0, stop=t == J1 - 1)
                    last.then_inc(mlp_full, 1)
                pe.wait_ge(mlp_copied, FILLS * c + J1 + J2)
                for t in range(J2):
                    last = pe.matmul(psM[0][0:1, :], w3[:, t:t + 1], hid2[:, t, :], start=t == 0, stop=t == J2 - 1)
                last.then_inc(mlp_full, 1)

            over_superchunks(pe, superchunk)


def _pair_rows():
    triangle = {}
    for f in range(FEATURES):
        for g in range(f + 1, FEATURES):
            triangle[f, g] = len(triangle)
    first_sd, first_pair = 128, 128 + FEATURES
    found = []
    for k in range(1, FEATURES + 1):
        for f in range(FEATURES + 1 - k):
            found.append(first_sd + f if f + k == FEATURES else first_pair + triangle[f, f + k])
    return found


def kernel(**inputs):
    import numpy as _np
    import concourse.bacc as _bacc
    from concourse import mybir as _mybir
    from concourse.bass_utils import run_bass_kernel_spmd as _run

    nc = _bacc.Bacc("TRN2", target_bir_lowering=False, num_devices=1)
    arrays = {}

    def given(name, a):
        a = _np.ascontiguousarray(a)
        arrays[f"in_{name}"] = a
        return nc.dram_tensor(f"in_{name}", a.shape, _mybir.dt.from_np(a.dtype), kind="ExternalInput").ap()

    own = {n: given(n, inputs[n]) for n in ["r_dense_features", "ids", "W_top1", "W_top2"]}
    own |= {n: given(n, _np.asarray(inputs[n]).reshape(-1, 128).T) for n in ["b_top1", "b_top2", "W_top3"]}
    tables = [given(f"tbl_{f}", inputs[f"tbl_{f}"]) for f in range(FEATURES)]
    w_pairs = given("W_pairs", _np.asarray(inputs["W_top1"])[_pair_rows()])
    out = nc.dram_tensor("out", (inputs["ids"].shape[0], 1), _mybir.dt.float32, kind="ExternalOutput").ap()
    dlrm_tower(nc, own["r_dense_features"], own["ids"], tables, w_pairs, own["W_top1"], own["b_top1"],
               own["W_top2"], own["b_top2"], own["W_top3"], out)
    return _run(nc, [arrays], core_ids=[0]).results[0]["out"]
```

```python
import concourse.bass as bass
from concourse import mybir
from contextlib import ExitStack

FEATURES = 26
SMALL_ROWS = 1000
SMALL = 8


def vector_order(table_rows):
    small = [f for f in range(FEATURES) if table_rows[f] == SMALL_ROWS][:SMALL]
    return [f for f in range(FEATURES) if f not in small] + [FEATURES] + small


def pair_tiles():
    v = FEATURES + 1
    return [[(a, (a + k) % v) for k in range(4 * t + 1, 4 * t + 5) for a in range(v)]
            + [(a, (a + 13) % v) for a in range(9 * t, 9 * t + 9)] for t in range(3)]


def dlrm_tower(nc: bass.Bass, dense, ids, small_ids, tables, w_pairs, w_top1, b_top1, w_top2, b_top2, w_top3, out):
    fp32, fp32r, i32 = mybir.dt.float32, mybir.dt.float32r, mybir.dt.int32
    ALU = mybir.AluOpType
    ACT = mybir.ActivationFunctionType

    B, D = dense.shape
    ORDER = vector_order([t.shape[0] for t in tables])
    V = len(ORDER)
    GATHERED = ORDER[:ORDER.index(FEATURES)]
    G = len(GATHERED)
    SMALLS = ORDER[G + 1:]
    P = 128
    CHUNK = 256
    NCHUNK = B // CHUNK
    Q = CHUNK // P
    S = 4
    PARTS = [(0, 0, 32), (1, 0, 64), (2, 32, 64), (2, 64, 96), (3, 64, S * V)]
    GROUPS = CHUNK // S
    SUBGROUPS = P // S
    BATCH = 8
    BATCHES = SUBGROUPS // BATCH
    KP = 125
    KS = SMALL_ROWS // KP
    HALF = KS // 2
    TILES = pair_tiles()
    KT, KR = len(TILES), len(TILES[0])
    VW = V + 13
    H1 = w_top1.shape[1]
    H2 = w_top2.shape[1]
    J1, J2 = H1 // P, H2 // P
    TGROUPS = [list(range(v, min(v + 4, G + 1))) for v in range(0, G + 1, 4)]
    NT = len(TGROUPS)
    NPAIRS = SMALL // 2
    FILLS = Q * NT + NPAIRS
    MLP_FILLS = 4

    def t_fill(m, q, t, last):
        return NPAIRS + FILLS * m + q * (NT + (0 if last else NPAIRS // 2)) + t

    def small_fill(m, pair):
        if isinstance(m, int) and m == 0:
            return pair
        return NPAIRS + FILLS * (m - 1) + (pair // 2 + 1) * NT + pair

    products = nc.dram_tensor("products", (NCHUNK, V * VW, S, GROUPS), fp32, kind="Internal").ap()

    ctx = ExitStack()
    with ctx:
        def sb(name, shape, dt=fp32):
            return ctx.enter_context(nc.sbuf_tensor(name, shape, dt))

        def pb(name, shape):
            return ctx.enter_context(nc.psum_tensor(name, shape, fp32))

        def sem(name):
            return ctx.enter_context(nc.semaphore(name))

        SLOTS = 2 * Q
        index = sb("index", [P, SLOTS, FEATURES], i32)
        rows = [sb(f"rows{n}", [P, (G + 1) * D]) for n in range(SLOTS)]
        vec = [sb(f"vec{u}", [D, CHUNK * V]) for u in range(2)]
        gram = sb("gram", [S * V, 2, V, GROUPS])
        pairs = sb("pairs", [KR, KT, CHUNK])
        table_hi = sb("table_hi", [KP, SMALL, KS * D], fp32r)
        table_lo = sb("table_lo", [KP, SMALL, KS * D], fp32r)
        wanted = sb("wanted", [P, SMALL, CHUNK], i32)
        row_of = sb("row_of", [P, KS])
        onehot = sb("onehot", [KP, 2, HALF, CHUNK], fp32r)
        ident = sb("ident", [P, P])
        w1p = sb("w1p", [KR, KT, H1])
        w1d = sb("w1d", [D, H1])
        b1 = sb("b1", [P, J1])
        w2 = sb("w2", [P, J1, H2])
        b2 = sb("b2", [P, J2])
        w3 = sb("w3", [P, J2])
        hid1 = sb("hid1", [P, J1, CHUNK])
        hid2 = sb("hid2", [P, J2, CHUNK])
        y = hid2[0:1, 0, :]
        STAGES = 4
        RAW = KS * D
        staged = [rows[Q + n // 2][:, n % 2 * RAW:(n % 2 + 1) * RAW] for n in range(STAGES)]
        w1a, w1b = staged[SMALL % STAGES][:, 0:H1], staged[SMALL % STAGES][:, H1:2 * H1]

        psT = [pb(f"psT{i}", [P, 512]) for i in range(2)]
        psG = [pb(f"psG{i}", [P, 2, 512]) for i in range(2)]
        psM = [pb(f"psM{i}", [P, 2, CHUNK]) for i in range(2)]

        ident_zero = sem("ident_zero")
        constants_ready = sem("constants_ready")
        w_loaded = sem("w_loaded")
        wd_ready = sem("wd_ready")
        staged_ready = [sem(f"staged_ready{n}") for n in range(STAGES)]
        hi_ready = sem("hi_ready")
        lo_ready = sem("lo_ready")
        wanted_ready = [sem(f"wanted_ready{i}") for i in range(2)]
        onehot_ready = sem("onehot_ready")
        onehot_used = sem("onehot_used")
        wanted_started = sem("wanted_started")
        gathers_started = sem("gathers_started")
        index_ready = [sem(f"index_ready{n}") for n in range(SLOTS)]
        dense_ready = [sem(f"dense_ready{n}") for n in range(SLOTS)]
        rows_ready = [[sem(f"rows_ready{n}_{t}") for t in range(NT)] for n in range(SLOTS)]
        t_full = sem("t_full")
        t_copied = sem("t_copied")
        gram_full = [sem(f"gram_full{i}") for i in range(2)]
        gram_copied = [sem(f"gram_copied{i}") for i in range(2)]
        gram_stored = sem("gram_stored")
        pairs_ready = sem("pairs_ready")
        mlp_full = sem("mlp_full")
        mlp_copied = sem("mlp_copied")
        y_stored = sem("y_stored")

        G_IN = BATCHES // 2
        STORES = 2 * S
        LOADS = 2 * KT

        block = ctx.enter_context(nc.Block())

        def over_chunks(eng, step):
            for u in range(2):
                step(u, u, u == 0, False)
            with eng.Fori(1, NCHUNK // 2 - 1) as c:
                for u in range(2):
                    step(2 * c + u, u, False, False)
            for u in range(2):
                step(NCHUNK - 2 + u, u, False, u == 1)

        @block.gpsimd
        def _(pool):
            def gather(m, u, q):
                n = Q * u + q
                pool.wait_ge(index_ready[n], 16 * (m // 2 + 1) if isinstance(m, int) else 16 * ((m - u) // 2 + 1))
                if not isinstance(m, int):
                    pool.sem_inc(gathers_started, 1)
                for v, f in enumerate(GATHERED):
                    pool.indirect_dma_start(
                        out=rows[n][:, v * D:(v + 1) * D], out_offset=None, in_=tables[f],
                        in_offset=bass.IndirectOffsetOnAxis(ap=index[:, n, f:f + 1], axis=0),
                    ).then_inc(rows_ready[n][v // 4], 16)

            def step(m, u, first, last):
                for q in range(Q):
                    if isinstance(m, int) and m < 2:
                        if m == 1 and q == 0:
                            pool.wait_ge(lo_ready, SMALL)
                            pool.wait_ge(wd_ready, 1)
                    else:
                        pool.wait_ge(t_full, t_fill(m - 2, q, NT - 1, False) + 1)
                    gather(m, u, q)

            pool.memset(ident[:, :], 0.0).then_inc(ident_zero, 1)
            pool.iota(row_of[:, :], pattern=[[1, KS]], base=0, channel_multiplier=KS,
                      allow_small_or_imprecise_dtypes=True).then_inc(constants_ready, 1)
            pool.wait_ge(ident_zero, 1)
            pool.affine_select(out=ident[:, :], in_=ident[:, :], compare_op=ALU.not_equal, fill=1.0,
                               base=0, pattern=[[-1, P]], channel_multiplier=1).then_inc(constants_ready, 1)
            over_chunks(pool, step)

        @block.sync
        def _(sp):
            def load_inputs(m, u, q):
                n = Q * u + q
                at = m * CHUNK + q * P
                sp.dma_start(index[:, n, :], ids[bass.ds(at, P), :]).then_inc(index_ready[n], 16)
                sp.dma_start(rows[n][:, G * D:], dense[bass.ds(at, P), :]).then_inc(dense_ready[n], 16)

            def load_wanted(m, i):
                h = SMALL // 2
                part = small_ids[i * h:(i + 1) * h, bass.ds(m * CHUNK, CHUNK)]
                sp.dma_start(wanted[:, i * h:(i + 1) * h, :], part.unsqueeze(0).broadcast_to([P, h, CHUNK]))\
                  .then_inc(wanted_ready[i], 16)

            def load_table(i):
                to = staged[i % STAGES]
                if i >= STAGES:
                    sp.wait_ge(lo_ready, i - STAGES + 1)
                if i < SMALL:
                    table = tables[SMALLS[i]].rearrange("(p k) d -> p (k d)", k=KS)
                    for p, n in ((0, 112), (112, KP - 112)):
                        sp.dma_start(to[p:p + n, :], table[p:p + n, :]).then_inc(staged_ready[i % STAGES], 16)
                else:
                    sp.dma_start(w1a, w_top1[0:D, :]).then_inc(staged_ready[i % STAGES], 16)
                    sp.dma_start(w1b, w_top1[w_top1.shape[0] - D:, :]).then_inc(staged_ready[i % STAGES], 16)

            def step(m, u, first, last):
                if first:
                    sp.dma_start(w1p[:, :, :], w_pairs.rearrange("(t r) n -> r t n", r=KR)).then_inc(w_loaded, 16)
                    sp.dma_start(w2[:, :, :], w_top2.rearrange("(t p) n -> p t n", p=P)).then_inc(w_loaded, 16)
                    sp.dma_start(b1[:, :], b_top1).then_inc(w_loaded, 16)
                    sp.dma_start(b2[:, :], b_top2).then_inc(w_loaded, 16)
                    sp.dma_start(w3[:, :], w_top3).then_inc(w_loaded, 16)
                    sp.wait_ge(lo_ready, SMALL)
                    sp.wait_ge(wd_ready, 1)
                    for q in range(Q):
                        load_inputs(1, 1, q)
                more = not (isinstance(m, int) and m >= NCHUNK - 2)
                for q in range(Q):
                    if more:
                        sp.wait_ge(t_full, t_fill(m, q, NT - 1, last) + 1)
                        load_inputs(m + 2, u, q)
                        sp.wait_ge(onehot_ready, 2 * SMALL * (m + 1) + (q + 1) * SMALL)
                        if not isinstance(m, int):
                            sp.sem_inc(wanted_started, 1)
                        load_wanted(m + 2, q)
                for i in range(2):
                    sp.wait_ge(gram_copied[i], Q * G_IN * (m + 1))
                for s in range(S):
                    to = products[m, :, s, :].rearrange("(a b) n -> a b n", b=VW)
                    for b, n in ((0, V), (V, VW - V)):
                        sp.dma_start(to[:, b:b + n, :], gram[V * s:V * (s + 1), s % 2, 0:n, :]).then_inc(gram_stored, 16)
                sp.wait_ge(gram_stored, 16 * STORES * (m + 1))
                if not first:
                    sp.wait_ge(mlp_full, MLP_FILLS * (m - 1) + 2)
                for t in range(KT):
                    for r, k, ks, a, n in ((0, 4 * t + 1, 4, 0, V), (4 * V, 13, 1, 9 * t, 9)):
                        base = products[m, a * (VW + 1) + k:a * (VW + 1) + k + 1, :, :]
                        size = S * GROUPS
                        part = bass.AP(tensor=base.tensor, offset=base.offset,
                                       ap=[[size, ks], [(VW + 1) * size, n], [1, size]])
                        sp.dma_start(pairs[r:r + ks * n, t, :], part).then_inc(pairs_ready, 16)

            for q in range(Q):
                load_inputs(0, 0, q)
            for i in range(2):
                load_wanted(0, i)
            for i in range(SMALL + 1):
                load_table(i)
            for i in range(2):
                sp.wait_ge(onehot_ready, (i + 1) * SMALL)
                load_wanted(1, i)
            over_chunks(sp, step)

        def copy_products(copy, u, q, h):
            at = q * SUBGROUPS + h * BATCH
            for s, p, end in PARTS:
                last = copy(gram[p:end, s % 2, :, at:at + BATCH].rearrange("a b (k n) -> a k n b", k=2),
                            psG[h % 2][p:end, :, 0:4 * S * V]
                            .rearrange("a k (n s b) -> a k n s b", n=4, s=S)[:, :, :, s, :])
            return last

        def places(u, q, v, n):
            return vec[u][:, q * P * V:(q + 1) * P * V].rearrange("d (b v) -> d v b", v=V)[:, v:v + n, :]

        @block.scalar
        def _(act):
            def copy(o, i):
                return act.activation(o, i, ACT.Copy)

            def copy_pair(m, u, pair):
                act.wait_ge(t_full, small_fill(m, pair) + 1)
                i = small_fill(0, pair) if isinstance(m, int) and m == 0 else (pair // 2 + 1) * NT + pair
                for q in range(Q):
                    last = copy(places(u, q, G + 1 + 2 * pair, 2),
                                psT[i % 2][:, :].rearrange("d (v q b) -> d q v b", v=2, q=Q)[:, q, :, :])
                return last

            def step(m, u, first, last):
                for q in range(Q):
                    for t, vs in enumerate(TGROUPS):
                        fill = t_fill(m, q, t, last)
                        i = (q * (NT + (0 if last else NPAIRS // 2)) + t) % 2
                        act.wait_ge(t_full, fill + 1)
                        copy(places(u, q, vs[0], len(vs)),
                             psT[i][:, 0:len(vs) * P].rearrange("d (v b) -> d v b", b=P)).then_inc(t_copied, 1)
                    if q == 1 and not first:
                        mlp(m - 1)
                    for h in range(1, BATCHES, 2):
                        if not last:
                            copy_pair(m + 1, 1 - u, q * NPAIRS // 2 + h // 2).then_inc(t_copied, 1)
                        act.wait_ge(gram_full[1], G_IN * (Q * m + q) + h // 2 + 1)
                        if q == 0 and h == 1 and not first:
                            act.wait_ge(gram_stored, 16 * STORES * m)
                        copy_products(copy, u, q, h).then_inc(gram_copied[1], 1)

            def mlp(m):
                if isinstance(m, int) and m == 0:
                    act.wait_ge(w_loaded, 16 * 5)
                for j in range(0, J1, 2):
                    act.wait_ge(mlp_full, MLP_FILLS * m + j // 2 + 1)
                    act.activation(hid1[:, j, :], psM[j // 2][:, 0, :], ACT.Relu, bias=b1[:, j:j + 1])
                    act.activation(hid1[:, j + 1, :], psM[j // 2][:, 1, :], ACT.Relu, bias=b1[:, j + 1:j + 2])\
                       .then_inc(mlp_copied, 1)
                act.wait_ge(mlp_full, MLP_FILLS * m + 3)
                if not (isinstance(m, int) and m == 0):
                    act.wait_ge(y_stored, 16 * m)
                act.activation(hid2[:, 0, :], psM[0][:, 0, :], ACT.Relu, bias=b2[:, 0:1])
                act.activation(hid2[:, 1, :], psM[0][:, 1, :], ACT.Relu, bias=b2[:, 1:2]).then_inc(mlp_copied, 1)
                act.wait_ge(mlp_full, MLP_FILLS * (m + 1))
                act.activation(y.rearrange("o (n s) -> o s n", s=S),
                               psM[1][0:1, 0, :].rearrange("o (s n) -> o s n", s=S), ACT.Copy).then_inc(mlp_copied, 1)
                act.wait_ge(mlp_copied, MLP_FILLS * (m + 1))
                act.dma_start(out[bass.ds(m * CHUNK, CHUNK), :].rearrange("b o -> o b"), y).then_inc(y_stored, 16)

            for i in range(SMALL):
                act.wait_ge(staged_ready[i % STAGES], 32 * (i // STAGES + 1))
                copy(table_hi[:, i, :], staged[i % STAGES][0:KP, :]).then_inc(hi_ready, 1)
            for pair in range(NPAIRS):
                copy_pair(0, 0, pair).then_inc(t_copied, 1)
            over_chunks(act, step)
            mlp(NCHUNK - 1)
            act.wait_ge(y_stored, 16 * NCHUNK)

        @block.vector
        def _(dve):
            def copy(o, i):
                return dve.tensor_copy(o, i)

            def split(i):
                dve.wait_ge(staged_ready[i % STAGES], 32 * (i // STAGES + 1))
                dve.wait_ge(hi_ready, i + 1)
                dve.tensor_tensor(table_lo[:, i, :], staged[i % STAGES][0:KP, :], table_hi[:, i, :].bitcast(fp32),
                                  ALU.subtract).then_inc(lo_ready, 1)

            def onehots(m, i):
                if i % (SMALL // 2) == 0:
                    dve.wait_ge(wanted_ready[i // (SMALL // 2)], 16 * (m + 1))
                for half in range(2):
                    if not (isinstance(m, int) and m == 0 and i == 0):
                        before, pair = (m - 1, NPAIRS - 1) if i == 0 else (m, (i - 1) // 2)
                        if i % 2 == 1:
                            dve.wait_ge(onehot_used, 3 * (NPAIRS * m + i // 2) + 1 + half)
                        elif half == 0:
                            dve.wait_ge(onehot_used, 3 * (NPAIRS * m + i // 2))
                        else:
                            dve.wait_ge(t_full, small_fill(before, pair) + 1)
                    for k in range(HALF):
                        o = half * HALF + k
                        last = dve.tensor_scalar(onehot[:, half, k, :], wanted[0:KP, i, :], row_of[0:KP, o:o + 1], None,
                                                 ALU.is_equal)
                    last.then_inc(onehot_ready, 1)

            dve.wait_ge(constants_ready, 2)
            for i in range(SMALL):
                split(i)
                onehots(0, i)
            dve.wait_ge(staged_ready[SMALL % STAGES], 32 * (SMALL // STAGES + 1))
            dve.tensor_tensor(w1d[:, :], w1a, w1b, ALU.add).then_inc(wd_ready, 1)

            def step(m, u, first, last):
                for q in range(Q):
                    for h in range(0, BATCHES, 2):
                        if not last:
                            onehots(m + 1, BATCHES * q + h)
                            onehots(m + 1, BATCHES * q + h + 1)
                        dve.wait_ge(gram_full[0], G_IN * (Q * m + q) + h // 2 + 1)
                        if q == 0 and h == 0 and not first:
                            dve.wait_ge(gram_stored, 16 * STORES * m)
                        copy_products(copy, u, q, h).then_inc(gram_copied[0], 1)

            over_chunks(dve, step)

        @block.tensor
        def _(pe):
            def look_up(m, i):
                fill = small_fill(m, i // 2)
                bank = (i // 2 if isinstance(m, int) and m == 0 else (i // 4 + 1) * NT + i // 2) % 2
                if i % 2 == 0 and not (isinstance(m, int) and m == 0 and i < 4):
                    pe.wait_ge(t_copied, fill - 1)
                if isinstance(m, int) and m == 0:
                    pe.wait_ge(lo_ready, i + 1)
                for half in range(2):
                    pe.wait_ge(onehot_ready, 2 * SMALL * m + 2 * i + half + 1)
                    for k in range(HALF):
                        o = half * HALF + k
                        for part in (table_hi, table_lo):
                            last = pe.matmul(psT[bank][:, i % 2 * CHUNK:(i % 2 + 1) * CHUNK],
                                             part[:, i, o * D:(o + 1) * D], onehot[:, half, k, :],
                                             start=o == 0 and part is table_hi, stop=o == KS - 1 and part is table_lo)
                    if i % 2 == 1 and half == 1:
                        last.then_inc(t_full, 1)
                    else:
                        last.then_inc(onehot_used, 1)

            def transposes(m, u, q, last_step):
                n = Q * u + q
                for t, vs in enumerate(TGROUPS):
                    fill = t_fill(m, q, t, last_step)
                    i = (q * (NT + (0 if last_step else NPAIRS // 2)) + t) % 2
                    loads = 16 * (m // 2 + 1) if isinstance(m, int) else 16 * ((m - u) // 2 + 1)
                    pe.wait_ge(rows_ready[n][t], loads * len([v for v in vs if v < G]))
                    if G in vs:
                        pe.wait_ge(dense_ready[n], loads)
                    pe.wait_ge(t_copied, fill - 1)
                    for v in vs:
                        last = pe.transpose(psT[i][:, v % 4 * P:(v % 4 + 1) * P], rows[n][:, v * D:(v + 1) * D], ident[:, :])
                    last.then_inc(t_full, 1)

            def batch_products(m, u, q, h):
                if not (isinstance(m, int) and m == 0 and q == 0 and h < 2):
                    pe.wait_ge(gram_copied[h % 2], G_IN * (Q * m + q) + h // 2)
                for g in range(BATCH):
                    at = (q * P + (h * BATCH + g) * S) * V
                    mine = vec[u][:, at:at + S * V]
                    last = pe.matmul(psG[h % 2][0:S * V, g // 4, g % 4 * S * V:(g % 4 + 1) * S * V], mine, mine,
                                     start=True, stop=True)
                last.then_inc(gram_full[h % 2], 1)

            def mlp(m, u):
                if isinstance(m, int) and m == 0:
                    pe.wait_ge(w_loaded, 16 * 5)
                    pe.wait_ge(wd_ready, 1)
                else:
                    pe.wait_ge(mlp_copied, MLP_FILLS * m)
                pe.wait_ge(pairs_ready, 16 * LOADS * (m + 1))
                for j in range(J1):
                    to = psM[j // 2][:, j % 2, :]
                    pe.matmul(to, w1d[:, j * P:(j + 1) * P], vec[u][:, :].rearrange("d (n s v) -> d s n v", s=S, v=V)[:, :, :, G],
                              start=True, stop=False)
                    for t in range(KT):
                        last = pe.matmul(to, w1p[:, t, j * P:(j + 1) * P], pairs[:, t, :], start=False, stop=t == KT - 1)
                    if j % 2 == 1:
                        last.then_inc(mlp_full, 1)
                pe.wait_ge(mlp_copied, MLP_FILLS * m + 2)
                for j in range(J2):
                    for t in range(J1):
                        last = pe.matmul(psM[0][:, j, :], w2[:, t, j * P:(j + 1) * P], hid1[:, t, :],
                                         start=t == 0, stop=t == J1 - 1)
                last.then_inc(mlp_full, 1)
                pe.wait_ge(mlp_copied, MLP_FILLS * m + 3)
                for t in range(J2):
                    last = pe.matmul(psM[1][0:1, 0, :], w3[:, t:t + 1], hid2[:, t, :], start=t == 0, stop=t == J2 - 1)
                last.then_inc(mlp_full, 1)

            def step(m, u, first, last):
                for q in range(Q):
                    transposes(m, u, q, last)
                    if q == 1 and not first:
                        mlp(m - 1, 1 - u)
                    for h in range(BATCHES):
                        if not last:
                            look_up(m + 1, BATCHES * q + h)
                        if h == 0:
                            pe.wait_ge(t_copied, t_fill(m, q, NT - 1, last) + 1)
                        batch_products(m, u, q, h)

            pe.wait_ge(constants_ready, 2)
            for i in range(SMALL):
                look_up(0, i)
            over_chunks(pe, step)
            mlp(NCHUNK - 1, 1)


def _pair_rows(table_rows):
    triangle = {}
    for f in range(FEATURES):
        for g in range(f + 1, FEATURES):
            triangle[f, g] = len(triangle)
    order = vector_order(table_rows)
    found = []
    for tile in pair_tiles():
        for a, b in tile:
            f, g = sorted((order[a], order[b]))
            found.append(128 + f if g == FEATURES else 128 + FEATURES + triangle[f, g])
    assert len(set(found)) == len(found) == len(triangle) + FEATURES
    return found


def kernel(**inputs):
    import numpy as _np
    import concourse.bacc as _bacc
    from concourse import mybir as _mybir
    from concourse.bass_utils import run_bass_kernel_spmd as _run

    nc = _bacc.Bacc("TRN2", target_bir_lowering=False, num_devices=1)
    arrays = {}

    def given(name, a):
        a = _np.ascontiguousarray(a)
        arrays[f"in_{name}"] = a
        return nc.dram_tensor(f"in_{name}", a.shape, _mybir.dt.from_np(a.dtype), kind="ExternalInput").ap()

    own = {n: given(n, inputs[n]) for n in ["r_dense_features", "ids", "W_top1", "W_top2"]}
    own |= {n: given(n, _np.asarray(inputs[n]).reshape(-1, 128).T) for n in ["b_top1", "b_top2", "W_top3"]}
    tables = [given(f"tbl_{f}", inputs[f"tbl_{f}"]) for f in range(FEATURES)]
    table_rows = [t.shape[0] for t in tables]
    small = vector_order(table_rows)[-SMALL:]
    small_ids = given("small_ids", _np.asarray(inputs["ids"]).T[small])
    w_pairs = given("W_pairs", _np.asarray(inputs["W_top1"])[_pair_rows(table_rows)])
    out = nc.dram_tensor("out", (inputs["ids"].shape[0], 1), _mybir.dt.float32, kind="ExternalOutput").ap()
    dlrm_tower(nc, own["r_dense_features"], own["ids"], small_ids, tables, w_pairs, own["W_top1"], own["b_top1"],
               own["W_top2"], own["b_top2"], own["W_top3"], out)
    return _run(nc, [arrays], core_ids=[0]).results[0]["out"]
```

```python
import concourse.bass as bass
from concourse import mybir
from contextlib import ExitStack

FEATURES = 26
SMALL_ROWS = 1000
SMALL = 7


def vector_order(table_rows):
    small = [f for f in range(FEATURES) if table_rows[f] == SMALL_ROWS][:SMALL]
    return [f for f in range(FEATURES) if f not in small] + [FEATURES] + small


def pair_blocks():
    n, half = FEATURES, FEATURES // 2
    return [[(4 * t + 1, 4, n + 1, n),
             [(half, 1, n + 1, half), (half + half * (n + 1), 1, n + 1, half), (n * (n + 1) - half, 1, 1, half)][t]]
            for t in range(3)]


def pair_tiles():
    return [[divmod(first + d + step * i, FEATURES) for first, sequences, step, length in blocks
             for d in range(sequences) for i in range(length)] for blocks in pair_blocks()]


def dlrm_tower(nc: bass.Bass, dense, ids, small_ids, tables, w_pairs, w_top1, b_top1, w_top2, b_top2, w_top3, out):
    fp32, fp32r, i32 = mybir.dt.float32, mybir.dt.float32r, mybir.dt.int32
    ALU = mybir.AluOpType
    ACT = mybir.ActivationFunctionType

    B, D = dense.shape
    ORDER = vector_order([t.shape[0] for t in tables])
    V = len(ORDER)
    W = V - 1
    GATHERED = ORDER[:ORDER.index(FEATURES)]
    G = len(GATHERED)
    SMALLS = ORDER[G + 1:]
    P = 128
    CHUNK = 256
    NCHUNK = B // CHUNK
    Q = CHUNK // P
    S = 4
    PARTS = [(0, 0, 32), (1, 0, 64), (2, 32, 64), (2, 64, 96), (3, 64, S * V)]
    GROUPS = CHUNK // S
    SUBGROUPS = P // S
    BATCH = 8
    BATCHES = SUBGROUPS // BATCH
    KP = 125
    KS = SMALL_ROWS // KP
    HALF = KS // 2
    TILES = pair_tiles()
    KT, KR = len(TILES), len(TILES[0])
    H1 = w_top1.shape[1]
    H2 = w_top2.shape[1]
    J1, J2 = H1 // P, H2 // P
    TGROUPS = [list(range(v, min(v + 4, G + 1))) for v in range(0, G + 1, 4)]
    NT = len(TGROUPS)
    NPAIRS = (SMALL + 1) // 2
    FIRST_SMALLS = SMALL - SMALL // 2
    QUARTERS = [[0], [1], [2], list(range(3, NT))]
    T_PLACE, PAIR_PLACE, HALF_FILLS = [], [], 0
    for h, ts in enumerate(QUARTERS):
        if h % 2 == 1:
            PAIR_PLACE.append(HALF_FILLS)
            HALF_FILLS += 1
        for t in ts:
            T_PLACE.append(HALF_FILLS)
            HALF_FILLS += 1
    MLP_FILLS = 4
    START_T = [[t for t in (2 * pair, 2 * pair + 1) if t < NT] for pair in range(NPAIRS)]
    START_PAIR = [pair + sum(len(ts) for ts in START_T[:pair]) for pair in range(NPAIRS)]

    def t_fill(m, q, t):
        if isinstance(m, int) and m == 0 and q == 0:
            return START_PAIR[t // 2] + 1 + t % 2
        alone = isinstance(m, int) and m == NCHUNK - 1 and q == 1
        return NPAIRS + NT + HALF_FILLS * (Q * m + q - 1) + (t if alone else T_PLACE[t])

    def looked_up(q, h):
        i = BATCHES * q + h
        return i if SMALL == Q * BATCHES or i < SMALL - 1 else {Q * BATCHES - 1: SMALL - 1}.get(i)

    def small_fill(m, pair):
        if isinstance(m, int) and m == 0:
            return START_PAIR[pair]
        return NPAIRS + NT + HALF_FILLS * (Q * (m - 1) + pair // 2) + PAIR_PLACE[pair % 2]

    def standing(m, u):
        return m if isinstance(m, int) else 2 + u

    def late(m, q):
        return isinstance(m, int) and m == NCHUNK - 2 and q == 1

    def following(m, u, q):
        if q + 1 < Q:
            return m, u, q + 1
        return None if isinstance(m, int) and m == NCHUNK - 1 else (m + 1, 1 - u, 0)

    products = nc.dram_tensor("products", (NCHUNK - 1 + Q, V * W * CHUNK), fp32, kind="Internal").ap()

    ctx = ExitStack()
    with ctx:
        def sb(name, shape, dt=fp32):
            return ctx.enter_context(nc.sbuf_tensor(name, shape, dt))

        def pb(name, shape):
            return ctx.enter_context(nc.psum_tensor(name, shape, fp32))

        def sem(name):
            return ctx.enter_context(nc.semaphore(name))

        SLOTS = 2 * Q
        index = sb("index", [P, SLOTS, FEATURES], i32)
        rows = [sb(f"rows{n}", [P, (G + 1) * D]) for n in range(Q)]
        vec = [sb(f"vec{u}", [D, CHUNK * V]) for u in range(2)]
        gram = [sb(f"gram{u}", [P, 2, W, GROUPS]) for u in range(2)]
        pairs = sb("pairs", [KR + 1, KT, CHUNK])
        last_pairs = rows[0][0:KR + 1, 0:KT * CHUNK].rearrange("r (t n) -> r t n", t=KT)
        table_hi = sb("table_hi", [KP, SMALL, KS * D], fp32r)
        table_lo = sb("table_lo", [KP, SMALL, KS * D], fp32r)
        wanted = sb("wanted", [P, SMALL, CHUNK], i32)
        row_of = sb("row_of", [P, KS])
        onehot = sb("onehot", [KP, 2, HALF, CHUNK], fp32r)
        ident = sb("ident", [P, P])
        w1p = sb("w1p", [KR + 1, KT, H1])
        w1d = sb("w1d", [D, H1])
        w2_hi = sb("w2_hi", [P, J1, H2], fp32r)
        w2_lo = sb("w2_lo", [P, J1, H2], fp32r)
        b2 = sb("b2", [P, J2])
        w3 = sb("w3", [P, J2])
        hid1_hi = sb("hid1_hi", [P, J1, CHUNK], fp32r)
        hid1_lo = sb("hid1_lo", [P, J1, CHUNK], fp32r)
        hid2 = sb("hid2", [P, J2, CHUNK])
        y = hid2[0:1, 0, :]
        STAGES = 4
        RAW = KS * D
        staged = [gram[n // 2][:, :, :, :].rearrange("p e v n -> p (e v n)")[:, n % 2 * RAW:(n % 2 + 1) * RAW]
                  for n in range(STAGES)]
        w2_raw = staged[(SMALL + 1) % STAGES].rearrange("p (t n) -> p t n", t=J1)
        w1a, w1b = staged[SMALL % STAGES][:, 0:H1], staged[SMALL % STAGES][:, H1:2 * H1]

        psT = [pb(f"psT{i}", [P, 512]) for i in range(2)]
        psG = [pb(f"psG{i}", [P, 2, 512]) for i in range(2)]
        psM = [pb(f"psM{i}", [P, 2, CHUNK]) for i in range(2)]

        ident_zero = sem("ident_zero")
        constants_ready = sem("constants_ready")
        w_loaded = sem("w_loaded")
        wd_ready = sem("wd_ready")
        w2_hi_ready = sem("w2_hi_ready")
        w2_ready = sem("w2_ready")
        ones_ready = sem("ones_ready")
        last_ones_ready = sem("last_ones_ready")
        staged_ready = [sem(f"staged_ready{n}") for n in range(STAGES)]
        hi_ready = sem("hi_ready")
        lo_ready = sem("lo_ready")
        wanted_ready = [sem(f"wanted_ready{i}") for i in range(2)]
        onehot_ready = sem("onehot_ready")
        onehot_used = sem("onehot_used")
        wanted_started = sem("wanted_started")
        gathers_started = sem("gathers_started")
        index_ready = [sem(f"index_ready{n}") for n in range(SLOTS)]
        dense_ready = [sem(f"dense_ready{q}") for q in range(Q)]
        rows_ready = [[sem(f"rows_ready{q}_{t}") for t in range(NT)] for q in range(Q)]
        t_full = sem("t_full")
        t_copied = sem("t_copied")
        gram_full = [sem(f"gram_full{i}") for i in range(2)]
        gram_copied = [sem(f"gram_copied{i}") for i in range(2)]
        gram_stored = sem("gram_stored")
        pairs_ready = sem("pairs_ready")
        mlp_full = sem("mlp_full")
        mlp_copied = sem("mlp_copied")
        hid1_split = sem("hid1_split")
        y_stored = sem("y_stored")

        G_IN = BATCHES // 2
        STORES = S
        LOADS = 2 * KT

        def layer1(m, h):
            return psG[h][:, 0, :].rearrange("p (k n) -> p k n", k=2) if isinstance(m, int) and m == NCHUNK - 1 else psM[h]

        block = ctx.enter_context(nc.Block())

        def over_chunks(eng, step, last_step=None):
            for u in range(2):
                step(u, u, u == 0, False)
            with eng.Fori(1, NCHUNK // 2 - 1) as c:
                for u in range(2):
                    step(2 * c + u, u, False, False)
            step(NCHUNK - 2, 0, False, False)
            if last_step:
                last_step(NCHUNK - 1, 1)
            else:
                step(NCHUNK - 1, 1, False, True)

        @block.gpsimd
        def _(pool):
            def gather(m, u, q):
                n = Q * u + q
                pool.wait_ge(index_ready[n], 16 * (m // 2 + 1) if isinstance(m, int) else 16 * ((m - u) // 2 + 1))
                for t, vs in enumerate(TGROUPS):
                    if not (isinstance(m, int) and m == 0):
                        pool.wait_ge(t_full, t_fill(m - 1, q, t) + 1)
                    if not isinstance(m, int):
                        pool.sem_inc(gathers_started, 1)
                    for v in vs:
                        if v < G:
                            pool.indirect_dma_start(
                                out=rows[q][:, v * D:(v + 1) * D], out_offset=None, in_=tables[GATHERED[v]],
                                in_offset=bass.IndirectOffsetOnAxis(ap=index[:, n, GATHERED[v]:GATHERED[v] + 1], axis=0),
                            ).then_inc(rows_ready[q][t], 16)

            def step(m, u, first, last):
                for q in range(Q):
                    gather(m, u, q)

            pool.memset(ident[:, :], 0.0).then_inc(ident_zero, 1)
            pool.memset(pairs[:, 0, :], 1.0).then_inc(ones_ready, 1)
            pool.iota(row_of[:, :], pattern=[[1, KS]], base=0, channel_multiplier=KS,
                      allow_small_or_imprecise_dtypes=True).then_inc(constants_ready, 1)
            pool.wait_ge(ident_zero, 1)
            pool.affine_select(out=ident[:, :], in_=ident[:, :], compare_op=ALU.not_equal, fill=1.0,
                               base=0, pattern=[[-1, P]], channel_multiplier=1).then_inc(constants_ready, 1)
            over_chunks(pool, step)

        @block.sync
        def _(sp):
            def load_index(m, u, q):
                at = m * CHUNK + q * P
                sp.dma_start(index[:, Q * u + q, :], ids[bass.ds(at, P), :]).then_inc(index_ready[Q * u + q], 16)

            def load_dense(m, q):
                at = m * CHUNK + q * P
                sp.dma_start(rows[q][:, G * D:], dense[bass.ds(at, P), :]).then_inc(dense_ready[q], 16)

            def load_wanted(m, i):
                a, b = ((0, FIRST_SMALLS), (FIRST_SMALLS, SMALL))[i]
                part = small_ids[a:b, bass.ds(m * CHUNK, CHUNK)]
                sp.dma_start(wanted[:, a:b, :], part.unsqueeze(0).broadcast_to([P, b - a, CHUNK]))\
                  .then_inc(wanted_ready[i], 16)

            def load_table(i):
                to = staged[i % STAGES]
                if i >= STAGES:
                    sp.wait_ge(lo_ready, i - STAGES + 1)
                if i < SMALL:
                    table = tables[SMALLS[i]].rearrange("(p k) d -> p (k d)", k=KS)
                    for p, n in ((0, 112), (112, KP - 112)):
                        sp.dma_start(to[p:p + n, :], table[p:p + n, :]).then_inc(staged_ready[i % STAGES], 16)
                elif i == SMALL:
                    sp.dma_start(w1a, w_top1[0:D, :]).then_inc(staged_ready[i % STAGES], 16)
                    sp.dma_start(w1b, w_top1[w_top1.shape[0] - D:, :]).then_inc(staged_ready[i % STAGES], 16)
                else:
                    for t in range(0, J1, 2):
                        sp.dma_start(w2_raw[:, t:t + 2, :], w_top2.rearrange("(t p) n -> p t n", p=P)[:, t:t + 2, :])\
                          .then_inc(staged_ready[i % STAGES], 16)

            def step(m, u, first, last):
                if first:
                    sp.dma_start(w1p[0:KR, :, :], w_pairs.rearrange("(t r) n -> r t n", r=KR)).then_inc(w_loaded, 16)
                    sp.dma_start(w1p[KR:KR + 1, 0, :], b_top1.unsqueeze(0)).then_inc(w_loaded, 16)
                    sp.dma_start(b2[:, :], b_top2).then_inc(w_loaded, 16)
                    sp.dma_start(w3[:, :], w_top3).then_inc(w_loaded, 16)
                more = not (isinstance(m, int) and m >= NCHUNK - 2)
                for q in range(Q):
                    if not last:
                        sp.wait_ge(t_full, t_fill(m, q, NT - 1) + 1)
                        load_dense(m + 1, q)
                    if more:
                        load_index(m + 2, u, q)
                        sp.wait_ge(onehot_ready, 2 * SMALL * (m + 1) + 2 * (FIRST_SMALLS, SMALL)[q])
                        if not isinstance(m, int):
                            sp.sem_inc(wanted_started, 1)
                        load_wanted(m + 2, q)
                for q in range(Q) if last else [None]:
                    through_dram(m, u, q)

            def through_dram(m, u, q):
                run, groups, samples = m, slice(None), slice(None)
                if q is not None:
                    run, groups, samples = m + q, slice(q * SUBGROUPS, (q + 1) * SUBGROUPS), slice(q * P, (q + 1) * P)
                size = CHUNK if q is None else P
                mine = products[run, 0:V * W * size]
                for i in range(2):
                    sp.wait_ge(gram_copied[i], G_IN * (Q * m + (Q if q is None else q + 1)))
                for s in range(S):
                    sp.dma_start(mine.rearrange("(a b s n) -> a b s n", a=V, b=W, s=S)[:, :, s, :],
                                 gram[u][V * s:V * (s + 1), s % 2, :, groups]).then_inc(gram_stored, 16)
                sp.wait_ge(gram_stored, 16 * STORES * (run + 1))
                to = pairs if q is None else last_pairs
                if isinstance(m, int) and m == 0:
                    sp.wait_ge(ones_ready, 1)
                elif q is not None:
                    sp.wait_ge(last_ones_ready, 1)
                    sp.wait_ge(pairs_ready, 16 * LOADS * run)
                else:
                    sp.wait_ge(mlp_full, MLP_FILLS * (m - 1) + 2)
                for t, blocks in enumerate(pair_blocks()):
                    r = 0
                    for start, sequences, row_step, n in blocks:
                        part = bass.AP(tensor=mine.tensor, offset=mine.offset + start * size,
                                       ap=[[size, sequences], [row_step * size, n], [1, size]])
                        sp.dma_start(to[r:r + sequences * n, t, samples], part).then_inc(pairs_ready, 16)
                        r += sequences * n

            load_index(0, 0, 0)
            load_wanted(0, 0)
            for i in range(2):
                load_table(i)
            load_index(0, 0, 1)
            load_dense(0, 0)
            load_wanted(0, 1)
            for i in range(2, STAGES):
                load_table(i)
            load_dense(0, 1)
            for i in range(STAGES, SMALL + 2):
                load_table(i)
            for q in range(Q):
                load_index(1, 1, q)
            for i in range(2):
                sp.wait_ge(onehot_ready, 2 * (FIRST_SMALLS, SMALL)[i])
                load_wanted(1, i)
            over_chunks(sp, step)

        def copy_products(copy, u, q, h):
            at = q * SUBGROUPS + h * BATCH
            for s, p, end in PARTS:
                last = copy(gram[u][p:end, s % 2, :, at:at + BATCH].rearrange("a b (k n) -> a k n b", k=2),
                            psG[h % 2][p:end, :, 0:4 * S * W]
                            .rearrange("a k (n s b) -> a k n s b", n=4, s=S)[:, :, :, s, :])
            return last

        def places(u, q, v, n):
            return vec[u][:, q * P * V:(q + 1) * P * V].rearrange("d (b v) -> d v b", v=V)[:, v:v + n, :]

        @block.scalar
        def _(act):
            def copy(o, i):
                return act.activation(o, i, ACT.Copy)

            def copy_pair(m, u, pair):
                act.wait_ge(t_full, small_fill(m, pair) + 1)
                i = small_fill(standing(m, u), pair)
                n = min(2, SMALL - 2 * pair)
                for q in range(Q):
                    last = copy(places(u, q, G + 1 + 2 * pair, n),
                                psT[i % 2][:, 0:n * CHUNK].rearrange("d (v q b) -> d q v b", v=n, q=Q)[:, q, :, :])
                return last

            def copy_transposes(m, u, q, t):
                act.wait_ge(t_full, t_fill(m, q, t) + 1)
                vs = TGROUPS[t]
                return copy(places(u, q, vs[0], len(vs)),
                            psT[t_fill(standing(m, u), q, t) % 2][:, 0:len(vs) * P].rearrange("d (v b) -> d v b", b=P))

            def mlp(m, h):
                if h == 0 and isinstance(m, int) and m == 0:
                    act.wait_ge(w_loaded, 16 * 4)
                act.wait_ge(mlp_full, MLP_FILLS * m + h + 1)
                if h < 2:
                    act.activation(hid1_hi[:, 2 * h:2 * h + 2, :], layer1(m, h)[:, :, :], ACT.Relu).then_inc(mlp_copied, 1)
                if h == 2:
                    if not (isinstance(m, int) and m == 0):
                        act.wait_ge(y_stored, 16 * m)
                    act.activation(hid2[:, 0, :], psM[0][:, 0, :], ACT.Relu, bias=b2[:, 0:1])
                    act.activation(hid2[:, 1, :], psM[0][:, 1, :], ACT.Relu, bias=b2[:, 1:2]).then_inc(mlp_copied, 1)
                if h == 3:
                    size = P if isinstance(m, int) and m == NCHUNK - 1 else CHUNK
                    for c in range(0, CHUNK, size):
                        copied = act.activation(y[:, c:c + size].rearrange("o (n s) -> o s n", s=S),
                                                psM[1][0:1, 0, c:c + size].rearrange("o (s n) -> o s n", s=S), ACT.Copy)
                    copied.then_inc(mlp_copied, 1)
                    act.wait_ge(mlp_copied, MLP_FILLS * (m + 1))
                    act.dma_start(out[bass.ds(m * CHUNK, CHUNK), :].rearrange("b o -> o b"), y).then_inc(y_stored, 16)

            def batch(m, u, q, h):
                act.wait_ge(gram_full[1], G_IN * (Q * m + q) + h // 2 + 1)
                if q == 0 and h == 1:
                    if isinstance(m, int) and m < 2:
                        act.wait_ge(lo_ready, SMALL)
                        act.wait_ge(wd_ready, 1)
                        act.wait_ge(w2_ready, 1)
                    else:
                        act.wait_ge(gram_stored, 16 * STORES * (m - 1))
                copy_products(copy, u, q, h).then_inc(gram_copied[1], 1)

            def step(m, u, first, last):
                for q in range(Q):
                    for h in range(BATCHES):
                        if h % 2 == 1:
                            if late(m, q):
                                batch(m, u, q, h)
                            copy_pair(m + 1, 1 - u, q * NPAIRS // 2 + h // 2).then_inc(t_copied, 1)
                        for t in QUARTERS[h]:
                            copy_transposes(*following(m, u, q), t).then_inc(t_copied, 1)
                        if q == 1 and not first and not (late(m, q) and h >= 2):
                            mlp(m - 1, h)
                        if h % 2 == 1 and not late(m, q):
                            batch(m, u, q, h)

            def last_step(m, u):
                mlp(m - 2, 2)
                for h in range(BATCHES):
                    if h % 2 == 1:
                        batch(m, u, 0, h)
                    if h == 0:
                        mlp(m - 2, 3)
                    if h == BATCHES - 1:
                        mlp(m - 1, 0)
                    copy_transposes(m, u, 1, h).then_inc(t_copied, 1)
                copy_transposes(m, u, 1, NT - 1).then_inc(t_copied, 1)
                for h in range(1, BATCHES, 2):
                    batch(m, u, 1, h)
                for h in range(1, MLP_FILLS):
                    mlp(m - 1, h)
                for h in range(MLP_FILLS):
                    mlp(m, h)

            def upper(i):
                act.wait_ge(staged_ready[i % STAGES], 32 * (i // STAGES + 1))
                copy(table_hi[:, i, :], staged[i % STAGES][0:KP, :]).then_inc(hi_ready, 1)

            for i in range(STAGES):
                upper(i)
            for pair in range(NPAIRS):
                copy_pair(0, 0, pair).then_inc(t_copied, 1)
                for t in START_T[pair]:
                    copy_transposes(0, 0, 0, t).then_inc(t_copied, 1)
                for i in range(STAGES + 2 * pair, min(STAGES + 2 * pair + 2, SMALL)):
                    upper(i)
            act.wait_ge(staged_ready[(SMALL + 1) % STAGES], 32 * ((SMALL + 1) // STAGES + 1))
            copy(w2_hi[:, :, :], w2_raw).then_inc(w2_hi_ready, 1)
            over_chunks(act, step, last_step)
            act.wait_ge(y_stored, 16 * NCHUNK)

        @block.vector
        def _(dve):
            def copy(o, i):
                return dve.tensor_copy(o, i)

            def split(i):
                dve.wait_ge(staged_ready[i % STAGES], 32 * (i // STAGES + 1))
                dve.wait_ge(hi_ready, i + 1)
                dve.tensor_tensor(table_lo[:, i, :], staged[i % STAGES][0:KP, :], table_hi[:, i, :].bitcast(fp32),
                                  ALU.subtract).then_inc(lo_ready, 1)

            def onehots(m, i):
                if i in (0, FIRST_SMALLS):
                    dve.wait_ge(wanted_ready[i // FIRST_SMALLS], 16 * (m + 1))
                used = (2 * SMALL - NPAIRS) * m + 3 * (i // 2)
                for half in range(2):
                    if not (isinstance(m, int) and m == 0 and i == 0):
                        if i % 2 == 1:
                            dve.wait_ge(onehot_used, used + 1 + half)
                        elif half == 0:
                            dve.wait_ge(onehot_used, used)
                        elif i == 0:
                            dve.wait_ge(t_full, small_fill(m - 1, NPAIRS - 1) + 1)
                        else:
                            dve.wait_ge(t_full, small_fill(m, i // 2 - 1) + 1)
                    for k in range(HALF):
                        o = half * HALF + k
                        last = dve.tensor_scalar(onehot[:, half, k, :], wanted[0:KP, i, :], row_of[0:KP, o:o + 1], None,
                                                 ALU.is_equal)
                    last.then_inc(onehot_ready, 1)

            dve.wait_ge(constants_ready, 2)
            onehots(0, 0)
            split(0)
            for i in range(1, SMALL):
                split(i)
                onehots(0, i)
            dve.wait_ge(staged_ready[SMALL % STAGES], 32 * (SMALL // STAGES + 1))
            dve.tensor_tensor(w1d[:, :], w1a, w1b, ALU.add).then_inc(wd_ready, 1)
            dve.wait_ge(w2_hi_ready, 1)
            dve.tensor_tensor(w2_lo[:, :, :], w2_raw, w2_hi[:, :, :].bitcast(fp32), ALU.subtract).then_inc(w2_ready, 1)

            def lower(m, h):
                dve.wait_ge(mlp_copied, MLP_FILLS * m + h + 1)
                dve.scalar_tensor_tensor(hid1_lo[:, 2 * h:2 * h + 2, :], layer1(m, h)[:, :, :], 0.0,
                                         hid1_hi[:, 2 * h:2 * h + 2, :].bitcast(fp32), ALU.max, ALU.subtract)\
                   .then_inc(hid1_split, 1)

            def batch(m, u, q, h):
                dve.wait_ge(gram_full[0], G_IN * (Q * m + q) + h // 2 + 1)
                if q == 0 and h == 0 and not (isinstance(m, int) and m < 2):
                    dve.wait_ge(gram_stored, 16 * STORES * (m - 1))
                copy_products(copy, u, q, h).then_inc(gram_copied[0], 1)

            def step(m, u, first, last):
                for q in range(Q):
                    for h in range(0, BATCHES, 2):
                        for g in (h, h + 1):
                            if looked_up(q, g) is not None:
                                onehots(m + 1, looked_up(q, g))
                            if q == 1 and g in (1, 2) and not first:
                                lower(m - 1, g - 1)
                            if late(m, q) and g == 2:
                                batch(m, u, q, h)
                        if not (late(m, q) and h == 2):
                            batch(m, u, q, h)

            def last_step(m, u):
                for h in range(0, BATCHES, 2):
                    batch(m, u, 0, h)
                dve.wait_ge(t_full, t_fill(m, 0, NT - 1) + 1)
                dve.memset(last_pairs[:, 0, :], 1.0).then_inc(last_ones_ready, 1)
                lower(m - 1, 0)
                for h in range(0, BATCHES, 2):
                    batch(m, u, 1, h)
                lower(m - 1, 1)
                for h in range(2):
                    lower(m, h)

            over_chunks(dve, step, last_step)

        @block.tensor
        def _(pe):
            def look_up(m, u, i):
                fill = small_fill(m, i // 2)
                bank = small_fill(standing(m, u), i // 2) % 2
                if i % 2 == 0 and not (isinstance(m, int) and m == 0 and i == 0):
                    pe.wait_ge(t_copied, fill - 1)
                if isinstance(m, int) and m == 0:
                    pe.wait_ge(lo_ready, i + 1)
                for half in range(2):
                    pe.wait_ge(onehot_ready, 2 * SMALL * m + 2 * i + half + 1)
                    for k in range(HALF):
                        o = half * HALF + k
                        for part in (table_hi, table_lo):
                            last = pe.matmul(psT[bank][:, i % 2 * CHUNK:(i % 2 + 1) * CHUNK],
                                             part[:, i, o * D:(o + 1) * D], onehot[:, half, k, :],
                                             start=o == 0 and part is table_hi, stop=o == KS - 1 and part is table_lo)
                    if (i % 2 == 1 or i == SMALL - 1) and half == 1:
                        last.then_inc(t_full, 1)
                    else:
                        last.then_inc(onehot_used, 1)

            def transposes(m, u, q, t):
                vs = TGROUPS[t]
                bank = t_fill(standing(m, u), q, t) % 2
                pe.wait_ge(rows_ready[q][t], 16 * (m + 1) * len([v for v in vs if v < G]))
                if G in vs:
                    pe.wait_ge(dense_ready[q], 16 * (m + 1))
                if not (isinstance(m, int) and m == 0 and q == 0 and t == 0):
                    pe.wait_ge(t_copied, t_fill(m, q, t) - 1)
                for v in vs:
                    last = pe.transpose(psT[bank][:, v % 4 * P:(v % 4 + 1) * P], rows[q][:, v * D:(v + 1) * D], ident[:, :])
                last.then_inc(t_full, 1)

            def batch_products(m, u, q, h):
                if not (isinstance(m, int) and m == 0 and q == 0 and h < 2):
                    pe.wait_ge(gram_copied[h % 2], G_IN * (Q * m + q) + h // 2)
                for g in range(BATCH):
                    at = (q * P + (h * BATCH + g) * S) * V
                    mine = vec[u][:, at:at + S * V]
                    last = pe.matmul(psG[h % 2][0:S * V, g // 4, g % 4 * S * W:(g % 4 + 1) * S * W], mine,
                                     mine.rearrange("d (s v) -> d s v", v=V)[:, :, 0:W], start=True, stop=True)
                last.then_inc(gram_full[h % 2], 1)

            def mlp(m, u, h, q=None):
                samples, groups, landed, mine = slice(None), slice(None), m + 1, pairs
                if q is not None:
                    mine = last_pairs
                    samples, groups, landed = slice(q * P, (q + 1) * P), slice(q * SUBGROUPS, (q + 1) * SUBGROUPS), m + 1 + q
                if h == 0:
                    if isinstance(m, int) and m == 0:
                        pe.wait_ge(w_loaded, 16 * 4)
                        pe.wait_ge(wd_ready, 1)
                    elif q == 0:
                        for i in range(2):
                            pe.wait_ge(gram_copied[i], G_IN * Q * (m + 1))
                    elif q is None:
                        pe.wait_ge(mlp_copied, MLP_FILLS * m)
                    pe.wait_ge(pairs_ready, 16 * LOADS * landed)
                if h < 2:
                    for j in range(2 * h, 2 * h + 2):
                        to = layer1(m, h)[:, j % 2, samples]
                        pe.matmul(to, w1d[:, j * P:(j + 1) * P],
                                  vec[u][:, :].rearrange("d (n s v) -> d s n v", s=S, v=V)[:, :, groups, G],
                                  start=True, stop=False)
                        for t in range(KT):
                            end = KR + 1 if t == 0 else KR
                            last = pe.matmul(to, w1p[0:end, t, j * P:(j + 1) * P], mine[0:end, t, samples],
                                             start=False, stop=t == KT - 1)
                if h == 2:
                    if isinstance(m, int) and m == 0:
                        pe.wait_ge(w2_ready, 1)
                    for j in range(J2):
                        for t in range(0, J1, 2):
                            if j == 0 and t == 0:
                                pe.wait_ge(hid1_split, 2 * m + 1)
                            elif j == 0:
                                pe.wait_ge(mlp_copied, MLP_FILLS * m + t // 2 + 1)
                            for w, x in ((w2_hi, hid1_hi), (w2_lo, hid1_hi), (w2_hi, hid1_lo)):
                                if j == 0 and x is hid1_lo:
                                    pe.wait_ge(hid1_split, 2 * m + t // 2 + 1)
                                for i in (t, t + 1):
                                    last = pe.matmul(psM[0][:, j, :], w[:, i, j * P:(j + 1) * P], x[:, i, :],
                                                     start=i == 0 and w is w2_hi and x is hid1_hi,
                                                     stop=i == J1 - 1 and x is hid1_lo)
                if h == 3:
                    pe.wait_ge(mlp_copied, MLP_FILLS * m + 3)
                    for t in range(J2):
                        last = pe.matmul(psM[1][0:1, 0, :], w3[:, t:t + 1], hid2[:, t, :], start=t == 0, stop=t == J2 - 1)
                if q != 0:
                    last.then_inc(mlp_full, 1)

            def subchunk_products(m, u, q, h):
                if h == 0:
                    pe.wait_ge(t_copied, t_fill(m, q, NT - 1) + 1)
                batch_products(m, u, q, h)

            def step(m, u, first, last):
                for q in range(Q):
                    for h in range(BATCHES):
                        if late(m, q) and h > 0:
                            subchunk_products(m, u, q, h)
                        if looked_up(q, h) is not None:
                            look_up(m + 1, 1 - u, looked_up(q, h))
                        if late(m, q) and h == 0:
                            subchunk_products(m, u, q, h)
                        for t in QUARTERS[h]:
                            transposes(*following(m, u, q), t)
                        if q == 1 and not first and not (late(m, q) and h >= 2):
                            mlp(m - 1, 1 - u, h)
                        if not late(m, q):
                            subchunk_products(m, u, q, h)

            def last_step(m, u):
                mlp(m - 2, u, 2)
                for h in range(BATCHES):
                    subchunk_products(m, u, 0, h)
                    if h == 0:
                        mlp(m - 2, u, 3)
                    if h == BATCHES - 1:
                        mlp(m - 1, 1 - u, 0)
                    transposes(m, u, 1, h)
                transposes(m, u, 1, NT - 1)
                for h in range(BATCHES):
                    subchunk_products(m, u, 1, h)
                mlp(m - 1, 1 - u, 1)
                for h in range(2):
                    mlp(m, u, h, 0)
                    mlp(m - 1, 1 - u, h + 2)
                for h in range(2):
                    mlp(m, u, h, 1)
                for h in range(2, MLP_FILLS):
                    mlp(m, u, h)

            pe.wait_ge(constants_ready, 2)
            for pair in range(NPAIRS):
                for i in range(2 * pair, min(2 * pair + 2, SMALL)):
                    look_up(0, 0, i)
                for t in START_T[pair]:
                    transposes(0, 0, 0, t)
            over_chunks(pe, step, last_step)


def _pair_rows(table_rows):
    triangle = {}
    for f in range(FEATURES):
        for g in range(f + 1, FEATURES):
            triangle[f, g] = len(triangle)
    order = vector_order(table_rows)
    found = []
    for tile in pair_tiles():
        for a, b in tile:
            f, g = sorted((order[a], order[b]))
            found.append(128 + f if g == FEATURES else 128 + FEATURES + triangle[f, g])
    assert len(set(found)) == len(found) == len(triangle) + FEATURES
    return found


def kernel(**inputs):
    import numpy as _np
    import concourse.bacc as _bacc
    from concourse import mybir as _mybir
    from concourse.bass_utils import run_bass_kernel_spmd as _run

    nc = _bacc.Bacc("TRN2", target_bir_lowering=False, num_devices=1)
    arrays = {}

    def given(name, a):
        a = _np.ascontiguousarray(a)
        arrays[f"in_{name}"] = a
        return nc.dram_tensor(f"in_{name}", a.shape, _mybir.dt.from_np(a.dtype), kind="ExternalInput").ap()

    own = {n: given(n, inputs[n]) for n in ["r_dense_features", "ids", "W_top1", "b_top1", "W_top2"]}
    own |= {n: given(n, _np.asarray(inputs[n]).reshape(-1, 128).T) for n in ["b_top2", "W_top3"]}
    tables = [given(f"tbl_{f}", inputs[f"tbl_{f}"]) for f in range(FEATURES)]
    table_rows = [t.shape[0] for t in tables]
    small = vector_order(table_rows)[-SMALL:]
    small_ids = given("small_ids", _np.asarray(inputs["ids"]).T[small])
    w_pairs = given("W_pairs", _np.asarray(inputs["W_top1"])[_pair_rows(table_rows)])
    out = nc.dram_tensor("out", (inputs["ids"].shape[0], 1), _mybir.dt.float32, kind="ExternalOutput").ap()
    dlrm_tower(nc, own["r_dense_features"], own["ids"], small_ids, tables, w_pairs, own["W_top1"], own["b_top1"],
               own["W_top2"], own["b_top2"], own["W_top3"], out)
    return _run(nc, [arrays], core_ids=[0]).results[0]["out"]
```
